# Optimizing a Trainium2 kernel written in Bass

```python
import numpy as np
import jax
import jax.numpy as jnp

def _softmax(x, axis=-1):
    return jax.nn.softmax(x, axis=axis)

def _gelu(x):
    return jax.nn.gelu(x, approximate=True)

def _silu(x):
    return jax.nn.silu(x)

def _sigmoid(x):
    return jax.nn.sigmoid(x)

def _layernorm(x, axis=-1, eps=1e-05):
    m = jnp.mean(x, axis=axis, keepdims=True)
    v = jnp.var(x, axis=axis, keepdims=True)
    return (x - m) / jnp.sqrt(v + eps)

def _scatter_add(tgt, idx, src, axis=0):
    return tgt.at[idx].add(src)

def _segment_sum(src, seg, n):
    return jax.ops.segment_sum(src, seg, n)
kernel_name = 'mk_perceiver_d1_seqx_r8_1e815f'

def setup_inputs(seed: int=0):
    np.random.seed(seed)
    _w = jnp.asarray

    def _rec_inputs():
        import jax
        import jax.numpy as jnp
        _rk = jax.random.key(seed)
        x = 0.0002417 + 0.9998 * jax.random.normal(jax.random.fold_in(_rk, 1), (64, 32, 128), jnp.float32)
        _lenS = 32 - jax.random.randint(jax.random.fold_in(_rk, 7), (64,), 0, max(1, 32 // 4) + 1, jnp.int32)
        _lenS2 = 257 - jax.random.randint(jax.random.fold_in(_rk, 8), (64,), 0, max(1, 257 // 4) + 1, jnp.int32)
        _ctx_1024P = jax.random.normal(jax.random.fold_in(_rk, 11), (64, 16, 128), jnp.float32)
        _ctx_1024c = jax.random.dirichlet(jax.random.fold_in(_rk, 511), 0.3 * jnp.ones((16,), jnp.float32), (64, 257))
        _ctx_1024t = jnp.einsum('bsk,bkd->bsd', _ctx_1024c, _ctx_1024P)
        _ctx_1024t = _ctx_1024t * jax.lax.rsqrt(jnp.mean(jnp.square(_ctx_1024t)) + 1e-12) * 0.953939
        ctx_1024 = 7.22013e-05 + 1.00017 * (_ctx_1024t + 0.3 * jax.random.normal(jax.random.fold_in(_rk, 611), (64, 257, 128), jnp.float32))
        _validS = jnp.arange(32)[None, :] < _lenS[:, None]
        _validS2 = jnp.arange(257)[None, :] < _lenS2[:, None]
        _causal = jnp.tril(jnp.ones((32, 32), dtype=bool))
        mask_Bx1xSxS2_ik1 = jnp.where(jnp.broadcast_to(_validS2[:, None, None, :], (64, 1, 32, 257)), 1, 0).astype(jnp.int32)
        return (x, ctx_1024, mask_Bx1xSxS2_ik1)
    x, ctx_1024, mask_Bx1xSxS2_ik1 = _rec_inputs()

    def _L0_xattn_setup():
        import jax, jax.numpy as jnp
        import numpy as np
        HEADS = 16
        EMBED = 128
        HEAD_DIM = EMBED // HEADS
        key = jax.random.key(seed)
        ks = jax.random.split(key, 6)
        N, S, E = (4, 256, EMBED)
        return {'value': jax.random.normal(ks[0], (N, S, E), dtype=jnp.float32), 'key': jax.random.normal(ks[1], (N, S, E), dtype=jnp.float32), 'query': jax.random.normal(ks[2], (N, S, E), dtype=jnp.float32), 'mask': jax.random.randint(ks[3], (N, 1, S, S), 0, 2, dtype=jnp.int32), 'w_out': jax.random.normal(ks[4], (E, E), dtype=jnp.float32) * E ** (-0.5), 'b_out': jax.random.normal(ks[5], (E,), dtype=jnp.float32) * 0.01}
    _L0_xattn_all = _L0_xattn_setup()
    _L0_xattn_in = {k: v for k, v in _L0_xattn_all.items() if k in ('w_out', 'b_out')}
    del _L0_xattn_all

    def _L0_attn_setup():
        import jax, jax.numpy as jnp
        import numpy as np
        D_MODEL = 128
        N_HEAD = 16
        D_HEAD = D_MODEL // N_HEAD
        N_CTX = 256
        ROPE_BASE = 10000.0
        SCALE = 1

        def _rope_cache(seq_len, d_head, dtype=jnp.float32):
            inv_freq = 1.0 / ROPE_BASE ** (jnp.arange(0, d_head, 2, dtype=jnp.float32) / d_head)
            t = jnp.arange(seq_len, dtype=jnp.float32)
            freqs = jnp.outer(t, inv_freq)
            emb = jnp.concatenate([freqs, freqs], -1)
            cos = jnp.cos(emb)[None, :, None, :].astype(dtype)
            sin = jnp.sin(emb)[None, :, None, :].astype(dtype)
            return (cos, sin)

        def _apply_rope(x, cos, sin):
            x_even = x[..., 0::2]
            x_odd = x[..., 1::2]
            x_rot = jnp.stack([-x_odd, x_even], axis=-1).reshape(x.shape)
            return x * cos + x_rot * sin

        def _rmsnorm(x, w):
            eps = jnp.finfo(x.dtype).eps
            var = jnp.mean(jnp.square(x), axis=-1, keepdims=True)
            return x * jax.lax.rsqrt(var + eps) * w
        key = jax.random.key(seed)
        ks = jax.random.split(key, 9)
        B, S = (2, N_CTX)
        x = jax.random.normal(ks[0], (B, S, D_MODEL), jnp.float32)
        s = 0.02
        Wq = jax.random.normal(ks[1], (D_MODEL, D_MODEL), jnp.float32) * s
        bq = jax.random.normal(ks[2], (D_MODEL,), jnp.float32) * s
        Wk = jax.random.normal(ks[3], (D_MODEL, D_MODEL), jnp.float32) * s
        bk = jax.random.normal(ks[4], (D_MODEL,), jnp.float32) * s
        Wv = jax.random.normal(ks[5], (D_MODEL, D_MODEL), jnp.float32) * s
        bv = jax.random.normal(ks[6], (D_MODEL,), jnp.float32) * s
        Wo = jax.random.normal(ks[7], (D_MODEL, D_MODEL), jnp.float32) * s
        norm_w = jnp.ones((D_HEAD,), jnp.float32)
        return {'x': x, 'Wq': Wq, 'bq': bq, 'Wk': Wk, 'bk': bk, 'Wv': Wv, 'bv': bv, 'Wo': Wo, 'norm_w': norm_w}
    _L0_attn_all = _L0_attn_setup()
    _L0_attn_in = {k: v for k, v in _L0_attn_all.items() if k in ('Wq', 'bq', 'Wk', 'bk', 'Wv', 'bv', 'Wo', 'norm_w')}
    del _L0_attn_all

    def _L0_ffn_setup():
        import jax, jax.numpy as jnp
        import numpy as np
        B, S, D, E, F = (2, 256, 128, 8, 512)
        key = jax.random.key(seed)
        ks = jax.random.split(key, 4)
        return {'hidden_states': jax.random.normal(ks[0], (B, S, D), dtype=jnp.float32), 'Wr': jax.random.normal(ks[1], (D, E), dtype=jnp.float32) * (1.0 / np.sqrt(D)), 'W1': jax.random.normal(ks[2], (E, D, F), dtype=jnp.float32) * (1.0 / np.sqrt(D)), 'b1': jnp.zeros((E, F), dtype=jnp.float32), 'W2': jax.random.normal(ks[3], (E, F, D), dtype=jnp.float32) * (1.0 / np.sqrt(F)), 'b2': jnp.zeros((E, D), dtype=jnp.float32)}
    _L0_ffn_all = _L0_ffn_setup()
    _L0_ffn_in = {k: v for k, v in _L0_ffn_all.items() if k in ('Wr', 'W1', 'b1', 'W2', 'b2')}
    del _L0_ffn_all
    return {'x': x, 'ctx_1024': ctx_1024, 'mask_Bx1xSxS2_ik1': mask_Bx1xSxS2_ik1, 'L0_xattn_w_out': _L0_xattn_in['w_out'], 'L0_xattn_b_out': _L0_xattn_in['b_out'], 'L0_attn_Wq': _L0_attn_in['Wq'], 'L0_attn_bq': _L0_attn_in['bq'], 'L0_attn_Wk': _L0_attn_in['Wk'], 'L0_attn_bk': _L0_attn_in['bk'], 'L0_attn_Wv': _L0_attn_in['Wv'], 'L0_attn_bv': _L0_attn_in['bv'], 'L0_attn_Wo': _L0_attn_in['Wo'], 'L0_attn_norm_w': _L0_attn_in['norm_w'], 'L0_ffn_Wr': _L0_ffn_in['Wr'], 'L0_ffn_W1': _L0_ffn_in['W1'], 'L0_ffn_b1': _L0_ffn_in['b1'], 'L0_ffn_W2': _L0_ffn_in['W2'], 'L0_ffn_b2': _L0_ffn_in['b2']}

def reference(x, ctx_1024, mask_Bx1xSxS2_ik1, L0_xattn_w_out, L0_xattn_b_out, L0_attn_Wq, L0_attn_bq, L0_attn_Wk, L0_attn_bk, L0_attn_Wv, L0_attn_bv, L0_attn_Wo, L0_attn_norm_w, L0_ffn_Wr, L0_ffn_W1, L0_ffn_b1, L0_ffn_W2, L0_ffn_b2):
    import jax
    import jax.numpy as jnp

    def _L0_xattn_ref(value, key, query, mask, w_out, b_out):
        import jax, jax.numpy as jnp
        import numpy as np
        HEADS = 16
        EMBED = 128
        HEAD_DIM = EMBED // HEADS
        N, Q, E = query.shape
        K = key.shape[1]
        H, D = (HEADS, HEAD_DIM)
        q = query.reshape(N, Q, H, D)
        k = key.reshape(N, K, H, D)
        v = value.reshape(N, K, H, D)
        energy = jnp.einsum('nqhd,nkhd->nhqk', q, k)
        energy = jnp.where(mask == 0, jnp.float32(-1e+22), energy)
        attn = jax.nn.softmax(energy / jnp.sqrt(jnp.float32(E)), axis=-1)
        out = jnp.einsum('nhqk,nkhd->nqhd', attn, v).reshape(N, Q, H * D)
        return out @ w_out.T + b_out

    def _L0_attn_ref(x, Wq, bq, Wk, bk, Wv, bv, Wo, norm_w):
        import jax, jax.numpy as jnp
        import numpy as np
        D_MODEL = 128
        N_HEAD = 16
        D_HEAD = D_MODEL // N_HEAD
        N_CTX = 256
        ROPE_BASE = 10000.0
        SCALE = 1

        def _rope_cache(seq_len, d_head, dtype=jnp.float32):
            inv_freq = 1.0 / ROPE_BASE ** (jnp.arange(0, d_head, 2, dtype=jnp.float32) / d_head)
            t = jnp.arange(seq_len, dtype=jnp.float32)
            freqs = jnp.outer(t, inv_freq)
            emb = jnp.concatenate([freqs, freqs], -1)
            cos = jnp.cos(emb)[None, :, None, :].astype(dtype)
            sin = jnp.sin(emb)[None, :, None, :].astype(dtype)
            return (cos, sin)

        def _apply_rope(x, cos, sin):
            x_even = x[..., 0::2]
            x_odd = x[..., 1::2]
            x_rot = jnp.stack([-x_odd, x_even], axis=-1).reshape(x.shape)
            return x * cos + x_rot * sin

        def _rmsnorm(x, w):
            eps = jnp.finfo(x.dtype).eps
            var = jnp.mean(jnp.square(x), axis=-1, keepdims=True)
            return x * jax.lax.rsqrt(var + eps) * w
        B, S, _ = x.shape
        split = lambda t: t.reshape(B, S, N_HEAD, D_HEAD)
        q = split(x @ Wq.T + bq)
        k = split(x @ Wk.T + bk)
        v = split(x @ Wv.T + bv)
        cos, sin = _rope_cache(S, D_HEAD, x.dtype)
        q = _apply_rope(_rmsnorm(q, norm_w), cos, sin)
        k = _apply_rope(_rmsnorm(k, norm_w), cos, sin)
        scores = jnp.einsum('bqhd,bkhd->bhqk', q, k)
        causal = jnp.tril(jnp.ones((S, S), x.dtype))
        pattern = jnp.square(scores / D_HEAD) * causal
        z = jnp.einsum('bhqk,bkhd->bqhd', pattern, v).reshape(B, S, D_MODEL)
        return x + z @ Wo.T * SCALE

    def _L0_ffn_ref(hidden_states, Wr, W1, b1, W2, b2):
        import jax, jax.numpy as jnp
        import numpy as np
        B, S, D, E, F = (2, 256, 128, 8, 512)
        b, s, d = hidden_states.shape
        e = Wr.shape[1]
        x = hidden_states.reshape(b * s, d)
        router_logits = x @ Wr
        router_probs = jax.nn.softmax(router_logits, axis=-1)
        expert_idx = jnp.argmax(router_probs, axis=-1)
        p_max = jnp.max(router_probs, axis=-1, keepdims=True)

        def expert_mlp(w1, bb1, w2, bb2):
            h = jax.nn.gelu(x @ w1 + bb1, approximate=False)
            return h @ w2 + bb2
        outs = jax.vmap(expert_mlp)(W1, b1, W2, b2)
        onehot = jax.nn.one_hot(expert_idx, e, dtype=x.dtype)
        next_states = jnp.einsum('te,etd->td', onehot, outs)
        out = p_max * next_states
        return out.reshape(b, s, d)
    x = x + _L0_xattn_ref(ctx_1024, ctx_1024, _layernorm(x, axis=-1), mask_Bx1xSxS2_ik1, L0_xattn_w_out, L0_xattn_b_out)
    x = x + _L0_attn_ref(_layernorm(x, axis=-1), L0_attn_Wq, L0_attn_bq, L0_attn_Wk, L0_attn_bk, L0_attn_Wv, L0_attn_bv, L0_attn_Wo, L0_attn_norm_w)
    x = x + _L0_ffn_ref(_layernorm(x, axis=-1), L0_ffn_Wr, L0_ffn_W1, L0_ffn_b1, L0_ffn_W2, L0_ffn_b2)
    return x

_drawn_inputs = setup_inputs


def setup_inputs(seed=0):
    import zlib

    import numpy as np

    out = dict(_drawn_inputs(seed))
    spreads = {'L0_attn_norm_w': (1.0, 0.6), 'L0_ffn_b1': (0.0, 0.652), 'L0_ffn_b2': (0.0, 0.448)}
    factors = {'L0_xattn_b_out': 3.674, 'L0_attn_bq': 8.0, 'L0_attn_bk': 8.0, 'L0_attn_bv': 5.398}
    for name, (base, spread) in spreads.items():
        noise = np.random.default_rng([zlib.crc32(name.encode()), seed]).standard_normal(out[name].shape)
        drawn = base * np.exp(spread * noise) if base else spread * noise
        out[name] = jnp.asarray(drawn.astype(out[name].dtype))
    for name, factor in factors.items():
        out[name] = (out[name] * factor).astype(out[name].dtype)
    return out
```

```python
import concourse.bass as bass
from concourse import mybir
from contextlib import ExitStack
import numpy as np

B, S, D = 64, 32, 128
SK = 257
H, DH = 16, 8
P = 128
GB = P // S
NT = B // GB
HG = H // 4
E, F = 8, 512
FC = F // P
ET = (B * S) // P + E - 1
LN_EPS = 1e-5
RMS_EPS = float(np.finfo(np.float32).eps)
XSCALE = float(np.float32(1.0) / np.sqrt(np.float32(D)))
BIG = 1.0035028776097996e22

CONST_PARTS = [("ident", P), ("head16", H), ("head4", 4), ("hsame", 32), ("causal", S), ("cos", DH), ("sin", DH),
               ("before", P), ("ones", P), ("pick", GB * P), ("diag16", 16), ("tileno", ET), ("rev", E), ("fill", NT)]
CONST_AT, _at = {}, 0
for _name, _n in CONST_PARTS:
    CONST_AT[_name] = (_at, _at + _n)
    _at += _n
CONST_N = _at


def const_table():
    t = np.zeros((P, CONST_N), np.float32)
    p = np.arange(P)

    def put(name, a):
        lo, hi = CONST_AT[name]
        t[:, lo:hi] = np.asarray(a, np.float32).reshape(P, hi - lo)

    put("ident", np.eye(P))
    put("head16", (p[:, None] // DH) == np.arange(H)[None])
    put("head4", ((p[:, None] % 32) // DH) == np.arange(4)[None])
    put("hsame", (p[:, None] // S) == (np.arange(32)[None] // DH))
    put("causal", (p[:, None] % S) <= np.arange(S)[None])
    inv = (np.float32(1.0) / np.float32(10000.0) ** (np.arange(0, DH, 2, dtype=np.float32) / np.float32(DH))).astype(np.float32)
    ang = np.outer((p % S).astype(np.float32), inv).astype(np.float32)
    ang = np.concatenate([ang, ang], -1)
    put("cos", np.cos(ang))
    sign = np.where(np.arange(DH) % 2 == 0, -1.0, 1.0)
    put("sin", (np.sin(ang) * sign[None])[:, np.arange(DH) ^ 1])
    put("before", p[:, None] < p[None, :])
    put("ones", np.ones((P, P)))
    pick = np.zeros((P, GB, P))
    for b in range(GB):
        for r in range(S):
            pick[b * S + r, b, np.arange(4) * S + r] = 1
    put("pick", pick)
    d16 = np.zeros((P, 16))
    d16[:16] = np.eye(16)
    put("diag16", d16)
    put("tileno", np.broadcast_to(np.arange(ET), (P, ET)))
    put("rev", np.broadcast_to(E - np.arange(E), (P, E)))
    put("fill", np.broadcast_to(np.arange(NT) * P, (P, NT)))
    return t


def perceiver_block(nc, x, ctx, mask, w_out_t, b_out, wqkv_t, bqkv, wo_t, norm_w, wr, w1, b1, w2, b2, consts, out, xs_dram, ys_dram):
    fp32, bf16, i32, u32 = mybir.dt.float32, mybir.dt.bfloat16, mybir.dt.int32, mybir.dt.uint32
    ALU = mybir.AluOpType
    ACT = mybir.ActivationFunctionType
    AX = mybir.AxisListType
    ds = bass.ds

    stack = ExitStack()
    with stack:
        def sb(name, shape, dt=fp32):
            return stack.enter_context(nc.sbuf_tensor(name, shape, dt))

        def sem(name):
            return stack.enter_context(nc.semaphore(name))

        def after(eng, s, value):
            if isinstance(value, int) and value <= 0:
                return
            eng.wait_ge(s, value)

        C = sb("C", [P, CONST_N])

        def const(name, rows=P):
            lo, hi = CONST_AT[name]
            return C[0:rows, lo:hi]

        ident = const("ident")
        X = sb("X", [P, NT, D])
        XB = sb("XB", [P, NT, D])
        bout_bc = sb("bout_bc", [P, D])
        wout_sb = sb("wout_sb", [P, D])
        stats = sb("stats", [P, NT, 6])
        s1 = sb("s1", [P, NT]); s2 = sb("s2", [P, NT]); s3 = sb("s3", [P, NT]); s4 = sb("s4", [P, NT]); s5 = sb("s5", [P, NT])
        mean = sb("mean", [P, NT]); var = sb("var", [P, NT]); rstd = sb("rstd", [P, NT])
        mhalf = sb("mhalf", [P, 512])
        kl_rows = sb("kl_rows", [B, D])
        KTL = sb("KTL", [P, B])
        VLR = sb("VLR", [16, NT, D])
        pick_bf = sb("pick_bf", [P, GB, P], bf16)
        area = [sb(f"area{k}", [P, 4096]) for k in range(2)]
        V = [area[1][:, 2048 + 1024 * u:3072 + 1024 * u].rearrange("p (k b d) -> p k b d", k=2, b=GB) for u in range(2)]
        MK = [sb(f"MK{u}", [P, SK], i32) for u in range(2)]
        MB = [sb(f"MB{u}", [P, SK], bf16) for u in range(2)]
        KT = [sb(f"KT{u}", [P, GB, SK]) for u in range(2)]
        XH = sb("XH", [P, D])
        QT = sb("QT", [P, P])
        QB = [area[0][:, 2048 * u:2048 * (u + 1)].rearrange("p (b h q) -> p b h q", b=GB, h=H) for u in range(2)]
        NM = [sb(f"NM{v}", [P, 4]) for v in range(2)]
        PR = [sb(f"PR{v}", [P, 4, SK + 1]) for v in range(2)]
        ZS = [sb(f"ZS{u}", [P, 16]) for u in range(2)]
        RZ = sb("RZ", [P, 16])
        A = sb("A", [P, 16, 32])
        PLG = [sb(f"PLG{u}", [P, 16]) for u in range(2)]
        PLS = sb("PLS", [16, P])
        VLX = sb("VLX", [16, GB, P])
        PT = [[area[1][:, 1024 * k + 512 * v:1024 * k + 512 * v + 512] for v in range(2)] for k in range(2)]
        OSB = sb("OSB", [P, 512])
        OM = sb("OM", [P, 4, P])

        wqkv_sb = sb("wqkv_sb", [P, 3 * D]); bqkv_bc = sb("bqkv_bc", [P, 3 * D]); wo_sb = sb("wo_sb", [P, D]); nw_bc = sb("nw_bc", [P, DH])
        cosw = sb("cosw", [P, DH]); sinw = sb("sinw", [P, DH])
        XN = [sb(f"XN{u}", [P, D]) for u in range(2)]
        XNT = [sb(f"XNT{u}", [P, P]) for u in range(2)]
        QKV = sb("QKV", [P, NT, 3 * D])
        SQ = area[0][:, :].rearrange("p (t n) -> p t n", t=NT)
        QKC = area[1][:, :].rearrange("p (t n) -> p t n", t=NT)
        MS = sb("MS", [P, NT * 2 * H]); RN = sb("RN", [P, NT * 2 * H])
        QKR = [sb(f"QKR{u}", [P, 2 * D]) for u in range(2)]
        VS = [sb(f"VS{u}", [P, D]) for u in range(2)]
        KS = [sb(f"KS{u}", [P, P]) for u in range(2)]
        QS = [sb(f"QS{u}", [P, GB, 4 * S]) for u in range(2)]
        PS = [sb(f"PS{u}", [P, 4, P]) for u in range(2)]
        PM = [sb(f"PM{u}", [P, 4, P]) for u in range(2)]
        OM2 = [sb(f"OM2{u}", [P, 4, P]) for u in range(2)]
        wr_sb = sb("wr_sb", [P, E])
        W1S = sb("W1S", [P, E, F]); W2S = sb("W2S", [P, E * FC, D])
        B1 = sb("B1", [P, E, F]); B2 = sb("B2", [P, E, D])
        zrow = sb("zrow", [P, D])
        LG = sb("LG", [P, NT, E]); LE = sb("LE", [P, NT, E]); LP = sb("LP", [P, NT, E]); OH = sb("OH", [P, NT, E])
        CA = sb("CA", [P, NT, E]); CB = sb("CB", [P, NT, E]); SL = sb("SL", [P, NT, E]); TOT = sb("TOT", [P, NT, E])
        r1 = sb("r1", [P, NT]); r2 = sb("r2", [P, NT]); pmax = sb("pmax", [P, NT]); slotf = sb("slotf", [P, NT]); slot = sb("slot", [P, NT], i32)
        CT = sb("CT", [P, E, NT]); ea = sb("ea", [P, E]); eb = sb("eb", [P, E]); nt_e = sb("nt_e", [P, E]); base = sb("base", [P, E])
        TE = sb("TE", [P, ET, E]); tef = sb("tef", [P, ET]); te = sb("te", [P, ET], i32)
        def shared(k, at, *shape):
            n = int(np.prod(shape))
            v = area[k][:, at:at + n]
            return v if len(shape) == 1 else v.rearrange("p (a b) -> p a b", a=shape[0])

        YG = shared(0, 0, NT, D)
        HB = [shared(0, 2048 + F * u, F) for u in range(2)]
        HGL = [shared(0, 3072 + F * u, F) for u in range(2)]
        HT = [shared(1, F * u, FC, P) for u in range(2)]
        XS = [shared(1, 1024 + D * u, D) for u in range(2)]
        XST = [shared(1, 1280 + P * u, P) for u in range(2)]
        YS = [shared(1, 1536 + D * u, D) for u in range(2)]

        R = stack.enter_context(nc.psum_tensor("R", [P, 4, 512], fp32))
        T, O, M = ([stack.enter_context(nc.psum_tensor(f"T{k}", [P, 512], fp32)) for k in range(2)],
                   stack.enter_context(nc.psum_tensor("O", [P, 512], fp32)),
                   stack.enter_context(nc.psum_tensor("M", [P, 512], fp32)))

        c_in = sem("c_in"); x_in = sem("x_in"); kl_in = sem("kl_in"); vl_in = sem("vl_in"); w_in = sem("w_in"); wb_in = sem("wb_in")
        moe_in = sem("moe_in")
        v_in = [[sem(f"v_in{h}{u}") for u in range(2)] for h in range(2)]
        mk_in = [sem(f"mk_in{u}") for u in range(2)]
        ln_st = sem("ln_st"); ln_a = sem("ln_a"); ln_b = sem("ln_b"); ln_c = sem("ln_c"); ln_var = sem("ln_var"); ln_eps = sem("ln_eps"); ln_pow = sem("ln_pow"); ln_rs = sem("ln_rs")
        mh_set = sem("mh_set"); xb_ready = sem("xb_ready"); pk_ready = sem("pk_ready")
        ktl_tr = sem("ktl_tr"); ktl_all = sem("ktl_all")
        rows_done = sem("rows_done"); max_done = sem("max_done"); exp_done = sem("exp_done")
        tr0 = sem("tr0"); tr1 = sem("tr1"); ev0 = sem("ev0"); ev1 = sem("ev1"); pv_done = sem("pv_done")
        mb_ready = sem("mb_ready"); xh_ready = sem("xh_ready"); ktl_ready = sem("ktl_ready")
        kt_tr = sem("kt_tr"); kt_ready = sem("kt_ready"); qt_tr = sem("qt_tr"); qt_ready = sem("qt_ready"); qb_ready = sem("qb_ready")
        plc = sem("plc"); plt = sem("plt"); pl_ready = sem("pl_ready"); vlx_ready = sem("vlx_ready"); left_done = sem("left_done")
        rz_done = sem("rz_done"); a_ready = sem("a_ready"); zm_done = sem("zm_done"); osb_ready = sem("osb_ready"); om_ready = sem("om_ready")
        y_done = sem("y_done"); x1_done = sem("x1_done")

        bw_in = sem("bw_in"); wexp_in = sem("wexp_in"); zr_set = sem("zr_set"); xs_zero = sem("xs_zero"); cw_ready = sem("cw_ready")
        xn_ready = sem("xn_ready"); xn_tr = sem("xn_tr"); xnt_ready = sem("xnt_ready"); qkv_done = sem("qkv_done"); qkv_ready = sem("qkv_ready"); xr_ready = sem("xr_ready")
        sq_ready = sem("sq_ready"); ms_sum = sem("ms_sum"); ms_ready = sem("ms_ready"); rn_ready = sem("rn_ready"); qkn_ready = sem("qkn_ready")
        sin_ready = sem("sin_ready"); cos_ready = sem("cos_ready")
        qkr_ready = sem("qkr_ready"); vs_ready = sem("vs_ready"); qk_tr = sem("qk_tr"); ks_ready = sem("ks_ready"); qs_ready = sem("qs_ready")
        s_done = sem("s_done"); ps_ready = sem("ps_ready"); pm_ready = sem("pm_ready"); z_done = sem("z_done"); om2_ready = sem("om2_ready")
        y2_done = sem("y2_done"); x2_done = sem("x2_done")
        xm_ready = sem("xm_ready"); xm_tr = sem("xm_tr"); xmt_ready = sem("xmt_ready"); lg_done = sem("lg_done"); lg_tiles = sem("lg_tiles")
        dve_step = sem("dve_step"); le_in = sem("le_in"); le_ready = sem("le_ready"); oh_ready = sem("oh_ready"); cnt_done = sem("cnt_done"); slot_ready = sem("slot_ready"); te_ready = sem("te_ready")
        scattered = sem("scattered"); xs_in = [sem(f"xs_in{u}") for u in range(2)]
        xs_tr = sem("xs_tr"); xst_ready = sem("xst_ready"); up_done = sem("up_done"); hb_ready = sem("hb_ready"); hg_ready = sem("hg_ready")
        ht_tr = sem("ht_tr"); ht_ready = sem("ht_ready"); down_done = sem("down_done"); ys_ready = sem("ys_ready"); ys_out = [sem(f"ys_out{u}") for u in range(2)]
        yg_in = [sem(f"yg_in{t}") for t in range(NT)]; res_ready = sem("res_ready"); out_sent = sem("out_sent")

        block = stack.enter_context(nc.Block())

        def tiles(eng, body, count=NT):
            body(0, 0)
            body(1, 1)
            with eng.Fori(1, count // 2) as i:
                body(2 * i, 0)
                body(2 * i + 1, 1)
            if count % 2:
                body(count - 1, 0)

        def groups(eng, body):
            body(-1, 1, False, True, False)
            body(0, 0, True, True, False)
            with eng.Fori(0, (NT - 2) // 2) as i:
                body(2 * i + 1, 1, True, True, True)
                body(2 * i + 2, 0, True, True, True)
            body(NT - 1, 1, True, False, True)
            body(NT, 0, False, False, True)

        def one(expr):
            return ds(expr, 1)

        @block.sync
        def _(sp):
            sp.dma_start(C[:, :], consts).then_inc(c_in, 16)
            sp.dma_start(X[:, :, :], x.rearrange("(t b) q d -> (b q) t d", b=GB)).then_inc(x_in, 16)
            sp.dma_start(kl_rows[:, :], ctx[:, SK - 1, :]).then_inc(kl_in, 16)

            def rows_of(v, n):
                return v.rearrange("(a n) -> a n", a=1).broadcast_to([P, n])

            def group(G, u, cur, nxt, prev):
                if nxt:
                    w = 1 - u
                    after(sp, mb_ready, G)
                    sp.dma_start(MK[w][:, :], mask[ds(4 * (G + 1), GB), 0, :, :].rearrange("b q k -> (b q) k")).then_inc(mk_in[w], 16)
                    for half in range(2):
                        after(sp, pv_done, 4 * G - 2 + 2 * half)
                        src = ctx[ds(4 * (G + 1) + 2 * half, 2), :, :]
                        for kt in range(2):
                            sp.dma_start(V[w][:, kt, 2 * half:2 * half + 2, :],
                                         src[:, kt * P:(kt + 1) * P, :].rearrange("b k d -> k b d")).then_inc(v_in[half][w], 16)
                if isinstance(G, int) and G == -1:
                    sp.dma_start(bout_bc[:, :], b_out.rearrange("(a n) -> a n", a=1).broadcast_to([P, D])).then_inc(wb_in, 16)
                    sp.dma_start(wout_sb[:, :], w_out_t).then_inc(w_in, 16)
                    sp.dma_start(wqkv_sb[:, :], wqkv_t).then_inc(bw_in, 16)
                    sp.dma_start(wo_sb[:, :], wo_t).then_inc(bw_in, 16)
                    sp.dma_start(bqkv_bc[:, :], rows_of(bqkv, 3 * D)).then_inc(bw_in, 16)
                    sp.dma_start(nw_bc[:, :], rows_of(norm_w, DH)).then_inc(bw_in, 16)
                    sp.dma_start(wr_sb[:, :], wr).then_inc(bw_in, 16)
                    sp.dma_start(B1[:, :, :], rows_of(b1.rearrange("e f -> (e f)"), E * F).rearrange("p (e f) -> p e f", e=E)).then_inc(wexp_in, 16)
                    sp.dma_start(B2[:, :, :], rows_of(b2.rearrange("e f -> (e f)"), E * D).rearrange("p (e f) -> p e f", e=E)).then_inc(wexp_in, 16)
                    sp.wait_ge(zr_set, 1)
                    sp.dma_start(xs_dram.rearrange("(j p) d -> p j d", p=P), zrow[:, :].rearrange("p (a d) -> p a d", a=1).broadcast_to([P, ET, D])).then_inc(xs_zero, 16)
                    for b in range(GB):
                        sp.dma_start(VLR[4 * b:4 * b + 4, :, :],
                                     ctx.rearrange("(t b) k d -> b k t d", b=GB)[b:b + 1, SK - 1, :, :].broadcast_to([4, NT, D])).then_inc(vl_in, 16)
            groups(sp, group)
            for e in range(2):
                sp.dma_start(W1S[:, 4 * e:4 * e + 4, :], w1[4 * e:4 * e + 4, :, :].rearrange("e d f -> d e f")).then_inc(wexp_in, 16)
            for e in range(2):
                sp.dma_start(W2S[:, 16 * e:16 * e + 16, :], w2[4 * e:4 * e + 4, :, :].rearrange("e (c f) d -> f (e c) d", c=FC)).then_inc(wexp_in, 16)
            sp.wait_ge(scattered, 16 * NT)

            def expert_io(j, u):
                after(sp, xs_tr, j - 1)
                sp.dma_start(XS[u][:, :], xs_dram[ds(P * j, P), :]).then_inc(xs_in[u], 16)
                if not (isinstance(j, int) and j < 2):
                    sp.wait_ge(ys_ready, j - 1)
                    sp.dma_start(ys_dram[ds(P * (j - 2), P), :], YS[u][:, :]).then_inc(ys_out[u], 16)
            tiles(sp, expert_io, ET)
            for j in (ET - 2, ET - 1):
                sp.wait_ge(ys_ready, j + 1)
                sp.dma_start(ys_dram[P * j:P * (j + 1), :], YS[j % 2][:, :]).then_inc(ys_out[j % 2], 16)
            for q in range(4):
                sp.wait_ge(res_ready, 4 * (q + 1))
                sp.dma_start(out.rearrange("(t b) q d -> (b q) t d", b=GB)[:, 4 * q:4 * q + 4, :], YG[:, 4 * q:4 * q + 4, :]).then_inc(out_sent, 16)
            sp.wait_ge(out_sent, 64)

        @block.vector
        def _(dve):
            def ln_stats(r):
                with dve.Fori(0, NT) as t:
                    nc.vector.bn_stats(stats[:, one(t), :], X[:, one(t), :]).then_inc(ln_st, 1)
                dve.wait_ge(ln_st, NT * (r + 1))
                me, ve, mo, vo = (stats[:, :, k] for k in (1, 2, 4, 5))
                nc.vector.tensor_tensor(s1[:, :], me, mo, ALU.add).then_inc(ln_a, 1)
                nc.vector.tensor_tensor(s2[:, :], me, mo, ALU.subtract).then_inc(ln_a, 1)
                nc.vector.tensor_tensor(s3[:, :], ve, vo, ALU.add).then_inc(ln_a, 1)
                dve.wait_ge(ln_a, 3 * (r + 1))
                nc.vector.tensor_scalar(mean[:, :], s1[:, :], 0.5, None, ALU.mult).then_inc(ln_b, 1)
                nc.vector.tensor_tensor(s4[:, :], s2[:, :], s2[:, :], ALU.mult).then_inc(ln_b, 1)
                nc.vector.tensor_scalar(s5[:, :], s3[:, :], 1.0 / D, LN_EPS, ALU.mult, ALU.add).then_inc(ln_b, 1)
                dve.wait_ge(ln_b, 3 * (r + 1))
                nc.vector.scalar_tensor_tensor(var[:, :], s4[:, :], 0.25, s5[:, :], ALU.mult, ALU.add).then_inc(ln_var, 1)

            dve.wait_ge(x_in, 16)
            ln_stats(0)
            dve.wait_ge(wb_in, 16)
            dve.wait_ge(c_in, 16)
            nc.vector.tensor_copy(pick_bf[:, :, :], const("pick").rearrange("p (b n) -> p b n", b=GB)).then_inc(pk_ready, 1)
            dve.wait_ge(ktl_tr, 1)
            nc.vector.tensor_copy(KTL[:, :], T[0][:, 0:B]).then_inc(ktl_all, 1)
            dve.wait_ge(ktl_all, 1)
            nc.vector.tensor_tensor(XB[:, :, :], X[:, :, :], bout_bc[:, :].rearrange("p (a d) -> p a d", a=1).broadcast_to([P, NT, D]), ALU.add).then_inc(xb_ready, 1)
            dve.wait_ge(ln_rs, 1)

            def group(G, u, cur, nxt, prev):
                w = 1 - u
                for s in range(GB):
                    n = 4 * G + s
                    if s == 3 and prev:
                        dve.wait_ge(zm_done, G)
                        dve.wait_ge(osb_ready, G)
                        nc.vector.tensor_tensor(OM[:, :, :].rearrange("p h (b q) -> p b h q", b=GB), OSB[:, :].rearrange("p (b h q) -> p b h q", b=GB, h=4),
                                                M[:, :].rearrange("p (b h q) -> p b h q", b=GB, h=4), ALU.mult).then_inc(om_ready, 1)
                    if cur:
                        for pair in range(2):
                            dve.wait_ge(rows_done, 4 * n + 2 * pair + 2)
                            nc.vector.tensor_reduce(NM[s % 2][:, 2 * pair:2 * pair + 2], R[:, 2 * pair:2 * pair + 2, 0:SK],
                                                    AX.X, ALU.max, negate=True).then_inc(max_done, 1)
                    if (cur if s else prev):
                        dve.wait_ge(tr1, n)
                        after(dve, pv_done, n - 2)
                        nc.vector.tensor_copy(PT[1][(s + 1) % 2][:, :], T[1][:, :]).then_inc(ev1, 1)
                    if s == 0 and nxt:
                        after(dve, rows_done, 16 * G)
                        dve.wait_ge(mk_in[w], 8 * (G + 3 - w))
                        nc.vector.tensor_scalar(MB[w][:, :], MK[w][:, :], 0.0, -BIG, ALU.is_equal, ALU.mult).then_inc(mb_ready, 1)
                        nc.vector.tensor_copy(KT[w][:, :, SK - 1], KTL[:, ds(4 * (G + 1), GB)]).then_inc(ktl_ready, 1)
                        after(dve, qt_tr, G + 1)
                        nc.vector.tensor_scalar(XH[:, :], X[:, one(G + 1), :], mean[:, one(G + 1)], rstd[:, one(G + 1)],
                                                ALU.subtract, ALU.mult).then_inc(xh_ready, 1)
                    if s == 1 and prev:
                        dve.wait_ge(exp_done, 16 * G)
                        nc.vector.reciprocal(RZ[:, :], ZS[w][:, :]).then_inc(rz_done, 1)
                        dve.wait_ge(plt, G)
                        if nxt:
                            dve.wait_ge(qt_tr, G + 2)
                        nc.vector.tensor_copy(PLS[:, :], M[0:16, 0:P]).then_inc(pl_ready, 1)
                        dve.wait_ge(rz_done, G)
                        nc.vector.tensor_tensor(A[:, :, :], RZ[:, :].rearrange("p (n a) -> p n a", a=1).broadcast_to([P, 16, 32]),
                                                const("hsame").rearrange("p (a n) -> p a n", a=1).broadcast_to([P, 16, 32]), ALU.mult).then_inc(a_ready, 1)
                    if s == 1 and nxt:
                        dve.wait_ge(qt_tr, G + 2)
                        after(dve, qb_ready, 4 * (G + 1))
                        nc.vector.tensor_copy(QT[:, :], M[:, P:2 * P]).then_inc(qt_ready, 1)
                    if s == 3 and prev:
                        dve.wait_ge(y_done, G)
                        nc.vector.tensor_tensor(X[:, one(G - 1), :], M[:, 0:D].rearrange("p (a d) -> p a d", a=1), XB[:, one(G - 1), :], ALU.add).then_inc(x1_done, 1)
            groups(dve, group)

            dve.wait_ge(x1_done, NT)
            ln_stats(1)
            dve.wait_ge(ln_rs, 2)
            dve.wait_ge(bw_in, 80)
            nc.vector.tensor_tensor(cosw[:, :], const("cos"), nw_bc[:, :], ALU.mult).then_inc(cw_ready, 1)
            nc.vector.tensor_tensor(sinw[:, :], const("sin"), nw_bc[:, :], ALU.mult).then_inc(cw_ready, 1)

            def project_in(t, u):
                after(dve, xn_tr, t - 1)
                nc.vector.tensor_scalar(XN[u][:, :], X[:, one(t), :], mean[:, one(t)], rstd[:, one(t)], ALU.subtract, ALU.mult).then_inc(xn_ready, 1)
                dve.wait_ge(xn_ready, t + 1)
                nc.vector.tensor_tensor(XB[:, one(t), :], X[:, one(t), :], XN[u][:, :].rearrange("p (a d) -> p a d", a=1), ALU.add).then_inc(xr_ready, 1)
                if not (isinstance(t, int) and t == 0):
                    dve.wait_ge(qkv_done, t)
                    nc.vector.tensor_tensor(QKV[:, one(t - 1), :], R[:, 1 - u:2 - u, 0:3 * D], bqkv_bc[:, :].rearrange("p (a n) -> p a n", a=1), ALU.add).then_inc(qkv_ready, 1)
            tiles(dve, project_in)
            dve.wait_ge(qkv_done, NT)
            nc.vector.tensor_tensor(QKV[:, NT - 1, :], R[:, 1, 0:3 * D], bqkv_bc[:, :], ALU.add).then_inc(qkv_ready, 1)

            hd = "p (n d) -> p n d"
            dve.wait_ge(sq_ready, 1)
            nc.vector.tensor_reduce(RN[:, :], SQ[:, :, :].rearrange("p t n -> p (t n)").rearrange(hd, d=DH), AX.X, ALU.add).then_inc(ms_sum, 1)
            dve.wait_ge(ms_sum, 1)
            nc.vector.tensor_scalar(MS[:, :], RN[:, :], 1.0 / DH, RMS_EPS, ALU.mult, ALU.add).then_inc(ms_ready, 1)
            dve.wait_ge(rn_ready, 1)
            nc.vector.tensor_tensor(QKC[:, :, :].rearrange("p t (n d) -> p t n d", d=DH), QKV[:, :, 0:2 * D].rearrange("p t (n d) -> p t n d", d=DH),
                                    RN[:, :].rearrange("p (t n a) -> p t n a", t=NT, a=1).broadcast_to([P, NT, 2 * H, DH]), ALU.mult).then_inc(qkn_ready, 1)
            dve.wait_ge(sin_ready, 1)
            qkc = QKC[:, :, :].rearrange("p t n -> p (t n)").rearrange(hd, d=DH)
            nc.vector.tensor_tensor(qkc, qkc, cosw[:, :].rearrange("p (a d) -> p a d", a=1).broadcast_to([P, NT * 2 * H, DH]), ALU.mult).then_inc(cos_ready, 1)
            dve.wait_ge(cos_ready, 1)

            def rotate(t, u):
                after(dve, qk_tr, t - 1)
                r = QKR[u][:, :].rearrange("p (a n two) -> p a n two", a=1, two=2)
                c = QKC[:, one(t), :].rearrange("p a (n two) -> p a n two", two=2)
                sn = SQ[:, one(t), :].rearrange("p a (n two) -> p a n two", two=2)
                for odd in range(2):
                    nc.vector.tensor_tensor(r[:, :, :, odd], c[:, :, :, odd], sn[:, :, :, 1 - odd], ALU.add).then_inc(qkr_ready, 1)

            def finish(t):
                dve.wait_ge(y2_done, t + 1)
                nc.vector.tensor_tensor(X[:, one(t), :], M[:, 0:D].rearrange("p (a d) -> p a d", a=1), XB[:, one(t), :], ALU.add).then_inc(x2_done, 1)

            def attend(t, u):
                if isinstance(t, int) and t == 0:
                    rotate(0, 0)
                dve.wait_ge(qk_tr, t + 1)
                h4 = const("head4").rearrange("p (h a) -> p h a", a=1)
                for b in range(GB):
                    nc.vector.tensor_tensor(QS[u][:, b, :].rearrange("p (h q) -> p h q", h=4),
                                            T[1][:, b * S:(b + 1) * S].rearrange("p (a q) -> p a q", a=1).broadcast_to([P, 4, S]),
                                            h4.broadcast_to([P, 4, S]), ALU.mult).then_inc(qs_ready, 1)
                if not (isinstance(t, int) and t == NT - 1):
                    rotate(t + 1, 1 - u)
                dve.wait_ge(ps_ready, t + 1)
                nc.vector.tensor_tensor(PM[u][:, :, :].rearrange("p g (h q) -> p (g h) q", q=S), PS[u][:, :, :].rearrange("p g (h q) -> p (g h) q", q=S),
                                        const("causal").rearrange("p (a q) -> p a q", a=1).broadcast_to([P, 16, S]), ALU.mult).then_inc(pm_ready, 1)
                if not (isinstance(t, int) and t == 0):
                    finish(t - 1)
                dve.wait_ge(z_done, t + 1)
                nc.vector.tensor_tensor(OM2[u][:, :, :].rearrange("p h (b q) -> p b h q", b=GB), R[:, :, 0:P].rearrange("p b (h q) -> p b h q", h=4),
                                        const("head4").rearrange("p (a h c) -> p a h c", a=1, c=1).broadcast_to([P, GB, 4, S]), ALU.mult).then_inc(om2_ready, 1)
            attend(0, 0)
            attend(1, 1)
            with dve.Fori(1, NT // 2 - 1) as i:
                attend(2 * i, 0)
                attend(2 * i + 1, 1)
            attend(NT - 2, 0)
            attend(NT - 1, 1)
            finish(NT - 1)

            dve.wait_ge(x2_done, NT)
            ln_stats(2)
            dve.wait_ge(ln_rs, 3)

            def routed_in(t, u):
                after(dve, xm_tr, t - 1)
                nc.vector.tensor_scalar(XN[u][:, :], X[:, one(t), :], mean[:, one(t)], rstd[:, one(t)], ALU.subtract, ALU.mult).then_inc(xm_ready, 1)
                nc.vector.tensor_scalar(XB[:, one(t), :], X[:, one(t), :], mean[:, one(t)], rstd[:, one(t)], ALU.subtract, ALU.mult).then_inc(xm_ready, 1)
            tiles(dve, routed_in)

            count = [0]

            def step(ins):
                count[0] += 1
                ins.then_inc(dve_step, 1)
                dve.wait_ge(dve_step, count[0])

            TT, TS, RED = nc.vector.tensor_tensor, nc.vector.tensor_scalar, nc.vector.tensor_reduce

            def per_e(v):
                return v[:, :].rearrange("p (t a) -> p t a", a=1).broadcast_to([P, NT, E])

            dve.wait_ge(lg_done, NT)
            step(nc.vector.tensor_copy(LG[:, :, :], O[:, 0:NT * E].rearrange("p (t e) -> p t e", e=E)))
            step(RED(r1[:, :], LG[:, :, :], AX.X, ALU.max))
            TT(LE[:, :, :], LG[:, :, :], per_e(r1), ALU.subtract).then_inc(le_in, 1)
            dve.wait_ge(le_ready, 1)
            step(RED(r2[:, :], LP[:, :, :], AX.X, ALU.add))
            step(nc.vector.reciprocal(r1[:, :], r2[:, :]))
            step(TT(LE[:, :, :], LP[:, :, :], per_e(r1), ALU.mult))
            step(RED(pmax[:, :], LE[:, :, :], AX.X, ALU.max))
            step(TT(LG[:, :, :], LE[:, :, :], per_e(pmax), ALU.is_equal))
            step(TT(LP[:, :, :], LG[:, :, :], const("rev").rearrange("p (a e) -> p a e", a=1).broadcast_to([P, NT, E]), ALU.mult))
            step(RED(r2[:, :], LP[:, :, :], AX.X, ALU.max))
            TT(OH[:, :, :], LP[:, :, :], per_e(r2), ALU.is_equal).then_inc(oh_ready, 1)
            dve.wait_ge(cnt_done, 1)
            nc.vector.tensor_copy(SL[:, :, :], M[:, 0:NT * E].rearrange("p (t e) -> p t e", e=E)).then_inc(dve_step, 1)
            count[0] += 1
            step(nc.vector.tensor_copy(TOT[:, :, :], T[0][:, 0:NT * E].rearrange("p (t e) -> p t e", e=E)))
            a, b = TOT, CA
            for k in (1, 2, 4, 8):
                nc.vector.tensor_copy(b[:, 0:k, :], a[:, 0:k, :]).then_inc(dve_step, 1)
                count[0] += 1
                step(TT(b[:, k:NT, :], a[:, k:NT, :], a[:, 0:NT - k, :], ALU.add))
                a, b = b, (CB if b is CA else CA)
            step(TT(b[:, :, :], a[:, :, :], TOT[:, :, :], ALU.subtract))
            step(TT(SL[:, :, :], SL[:, :, :], b[:, :, :], ALU.add))
            step(TT(CT[:, :, :], a[:, NT - 1, :].rearrange("p (e a) -> p e a", a=1).broadcast_to([P, E, NT]),
                    const("fill").rearrange("p (a t) -> p a t", a=1).broadcast_to([P, E, NT]), ALU.is_gt))
            step(RED(nt_e[:, :], CT[:, :, :], AX.X, ALU.add))
            a, b = nt_e, ea
            for k in (1, 2, 4):
                nc.vector.tensor_copy(b[:, 0:k], a[:, 0:k]).then_inc(dve_step, 1)
                count[0] += 1
                step(TT(b[:, k:E], a[:, k:E], a[:, 0:E - k], ALU.add))
                a, b = b, (eb if b is ea else ea)
            step(TT(b[:, :], a[:, :], nt_e[:, :], ALU.subtract))
            step(TS(base[:, :], b[:, :], float(P), None, ALU.mult))
            step(TT(SL[:, :, :], SL[:, :, :], base[:, :].rearrange("p (a e) -> p a e", a=1).broadcast_to([P, NT, E]), ALU.add))
            step(TT(SL[:, :, :], SL[:, :, :], OH[:, :, :], ALU.mult))
            step(RED(slotf[:, :], SL[:, :, :], AX.X, ALU.add))
            nc.vector.tensor_copy(slot[:, :], slotf[:, :]).then_inc(slot_ready, 1)
            step(TT(TE[:, :, :], a[:, :].rearrange("p (a e) -> p a e", a=1).broadcast_to([P, ET, E]),
                    const("tileno").rearrange("p (j a) -> p j a", a=1).broadcast_to([P, ET, E]), ALU.is_le))
            step(RED(tef[:, :], TE[:, :, :], AX.X, ALU.add))
            nc.vector.tensor_scalar(te[:, :], tef[:, :], float(E - 1), None, ALU.min).then_inc(te_ready, 1)
            dve.wait_ge(te_ready, 1)
            dve.wait_ge(wexp_in, 96)

            def hidden(j, u):
                e = dve.value_load(te[0:1, one(j)], min_val=0, max_val=E - 1)
                dve.wait_ge(up_done, j + 1)
                after(dve, hg_ready, j - 1)
                nc.vector.tensor_tensor(HB[u][:, :].rearrange("p (a f) -> p a f", a=1), R[:, u:u + 1, :], B1[:, one(e), :], ALU.add).then_inc(hb_ready, 1)

            def gathered(j, u):
                e = dve.value_load(te[0:1, one(j)], min_val=0, max_val=E - 1)
                dve.wait_ge(ht_tr, j + 1)
                after(dve, down_done, j - 1)
                nc.vector.tensor_copy(HT[u][:, :, :], R[:, 2 + u, :].rearrange("p (c n) -> p c n", c=FC)).then_inc(ht_ready, 1)
                dve.wait_ge(down_done, j + 1)
                if not (isinstance(j, int) and j < 2):
                    dve.wait_ge(ys_out[u], 8 * (j - u))
                nc.vector.tensor_tensor(YS[u][:, :].rearrange("p (a d) -> p a d", a=1), (O, M)[u][:, 0:D].rearrange("p (a d) -> p a d", a=1), B2[:, one(e), :], ALU.add).then_inc(ys_ready, 1)

            def expert(j, u):
                hidden(j, u)
                if not (isinstance(j, int) and j == 0):
                    gathered(j - 1, 1 - u)
            tiles(dve, expert, ET)
            gathered(ET - 1, 0)
            for t in range(NT):
                dve.wait_ge(yg_in[t], 16)
                nc.vector.scalar_tensor_tensor(YG[:, t, :], YG[:, t, :], pmax[:, t:t + 1], X[:, t, :], ALU.mult, ALU.add).then_inc(res_ready, 1)

        @block.scalar
        def _(act):
            def group(G, u, cur, nxt, prev):
                w = 1 - u
                for s in range(GB):
                    n = 4 * G + s
                    if cur:
                        after(act, tr1, n - 1)
                        after(act, plc, n - 1)
                        for g in range(4):
                            act.wait_ge(max_done, 2 * n + g // 2 + 1)
                            nc.scalar.activation(PR[s % 2][:, g, 0:SK], R[:, g, 0:SK], ACT.Exp, bias=NM[s % 2][:, g:g + 1],
                                                 accum_out=ZS[u][:, 4 * s + g:4 * s + g + 1]).then_inc(exp_done, 1)
                    if (cur if s else prev):
                        act.wait_ge(tr0, n)
                        after(act, pv_done, n - 2)
                        nc.scalar.activation(PT[0][(s + 1) % 2][:, :], T[0][:, :], ACT.Copy).then_inc(ev0, 1)
                    if s == 0 and cur:
                        act.wait_ge(kt_tr, 2 * G + 2)
                        nc.scalar.activation(KT[u][:, 2:4, 0:2 * P], M[:, :].rearrange("p (b k) -> p b k", b=2), ACT.Copy).then_inc(kt_ready, 1)
                    if s == 3 and nxt:
                        act.wait_ge(kt_tr, 2 * G + 3)
                        nc.scalar.activation(KT[w][:, 0:2, 0:2 * P], M[:, :].rearrange("p (b k) -> p b k", b=2), ACT.Copy).then_inc(kt_ready, 1)
                    if s == 1 and prev:
                        act.wait_ge(left_done, G)
                        nc.scalar.activation(OSB[:, :], O[:, :], ACT.Copy).then_inc(osb_ready, 1)
            groups(act, group)

            def transposed(t, u):
                act.wait_ge(xn_tr, t + 1)
                after(act, qkv_done, t - 1)
                nc.scalar.activation(XNT[u][:, :], T[u][:, 0:P], ACT.Copy).then_inc(xnt_ready, 1)
            tiles(act, transposed)
            act.wait_ge(qkv_ready, NT)
            nc.scalar.activation(SQ[:, :, :], QKV[:, :, 0:2 * D], ACT.Square).then_inc(sq_ready, 1)

            def attend(t, u):
                after(act, z_done, t - 1)
                nc.scalar.activation(VS[u][:, :].rearrange("p (a d) -> p a d", a=1), QKV[:, one(t), 2 * D:3 * D], ACT.Copy).then_inc(vs_ready, 1)
                act.wait_ge(qk_tr, t + 1)
                nc.scalar.activation(KS[u][:, :], T[0][:, 0:P], ACT.Copy).then_inc(ks_ready, 1)
                act.wait_ge(s_done, t + 1)
                nc.scalar.activation(PS[u][:, :, :], R[:, :, 0:P], ACT.Square, scale=1.0 / DH).then_inc(ps_ready, 1)
            tiles(act, attend)

            def router_in(t, u):
                act.wait_ge(xm_tr, t + 1)
                after(act, lg_done, t - 1)
                nc.scalar.activation(XNT[u][:, :], T[u][:, 0:P], ACT.Copy).then_inc(xmt_ready, 1)
            tiles(act, router_in)
            act.wait_ge(le_in, 1)
            nc.scalar.activation(LP[:, :, :], LE[:, :, :], ACT.Exp).then_inc(le_ready, 1)

            def expert(j, u):
                act.wait_ge(xs_tr, j + 1)
                after(act, up_done, j - 1)
                nc.scalar.activation(XST[u][:, :], T[u][:, 0:P], ACT.Copy).then_inc(xst_ready, 1)
                act.wait_ge(hb_ready, j + 1)
                after(act, ht_tr, j - 1)
                nc.scalar.activation(HGL[u][:, :], HB[u][:, :], ACT.Gelu).then_inc(hg_ready, 1)
            tiles(act, expert, ET)

        @block.gpsimd
        def _(pool):
            nc.gpsimd.memset(zrow[:, :], 0.0).then_inc(zr_set, 1)
            nc.gpsimd.memset(mhalf[:, :], -0.5).then_inc(mh_set, 1)
            pool.wait_ge(mh_set, 1)
            pool.wait_ge(ln_var, 1)
            nc.gpsimd.tensor_tensor(s4[:, :], var[:, :], mhalf[:, 0:NT], ALU.pow).then_inc(ln_pow, 1)
            pool.wait_ge(ln_pow, 1)
            nc.gpsimd.tensor_scalar(rstd[:, :], s4[:, :], XSCALE, None, ALU.mult).then_inc(ln_rs, 1)
            pool.wait_ge(c_in, 16)
            pool.wait_ge(vl_in, 64)

            def group(G, u, cur, nxt, prev):
                w = 1 - u
                for s in range(GB):
                    n = 4 * G + s
                    if cur:
                        pool.wait_ge(exp_done, 4 * n + 4)
                        nc.gpsimd.tensor_tensor(PLG[u][:, 4 * s:4 * s + 4], PR[s % 2][:, :, SK - 1], const("ones")[:, 0:4], ALU.mult).then_inc(plc, 1)
                    if s == 0 and prev:
                        nc.gpsimd.tensor_tensor(VLX[:, :, :].rearrange("p b (g c) -> p b g c", g=4),
                                                VLR[:, one(G - 1), :].rearrange("p a (g c) -> p a g c", g=4).broadcast_to([16, GB, 4, 32]),
                                                const("diag16", 16).rearrange("p (b g a) -> p b g a", b=GB, a=1).broadcast_to([16, GB, 4, 32]),
                                                ALU.mult).then_inc(vlx_ready, 1)
                    if s >= 2 and nxt:
                        if s == 2:
                            pool.wait_ge(qt_ready, G + 2)
                            after(pool, rows_done, 16 * G)
                        for b in (2 * s - 4, 2 * s - 3):
                            nc.gpsimd.tensor_tensor(QB[w][:, b, :, :],
                                                    QT[:, b * S:(b + 1) * S].rearrange("p (a q) -> p a q", a=1).broadcast_to([P, H, S]),
                                                    const("head16").rearrange("p (h a) -> p h a", a=1).broadcast_to([P, H, S]),
                                                    ALU.mult).then_inc(qb_ready, 1)
            groups(pool, group)

            pool.wait_ge(ln_var, 2)
            nc.gpsimd.tensor_tensor(rstd[:, :], var[:, :], mhalf[:, 0:NT], ALU.pow).then_inc(ln_rs, 1)
            pool.wait_ge(ms_ready, 1)
            nc.gpsimd.tensor_tensor(RN[:, :], MS[:, :], mhalf[:, :], ALU.pow).then_inc(rn_ready, 1)
            pool.wait_ge(qkn_ready, 1)
            pool.wait_ge(cw_ready, 2)
            flat = "p t (n d) -> p (t n) d"
            nc.gpsimd.tensor_tensor(SQ[:, :, :].rearrange(flat, d=DH), QKC[:, :, :].rearrange(flat, d=DH),
                                    sinw[:, :].rearrange("p (a d) -> p a d", a=1).broadcast_to([P, NT * 2 * H, DH]), ALU.mult).then_inc(sin_ready, 1)

            pool.wait_ge(ln_var, 3)
            nc.gpsimd.tensor_tensor(rstd[:, :], var[:, :], mhalf[:, 0:NT], ALU.pow).then_inc(ln_rs, 1)
            pool.wait_ge(xs_zero, 16)
            pool.wait_ge(slot_ready, 1)
            for t in range(NT):
                nc.gpsimd.indirect_dma_start(xs_dram, bass.IndirectOffsetOnAxis(ap=slot[:, t:t + 1].bitcast(u32), axis=0), XB[:, t, :], None).then_inc(scattered, 16)
            pool.wait_ge(ys_out[0], 16 * ((ET + 1) // 2))
            pool.wait_ge(ys_out[1], 16 * (ET // 2))
            for t in range(NT):
                nc.gpsimd.indirect_dma_start(YG[:, t, :], None, ys_dram, bass.IndirectOffsetOnAxis(ap=slot[:, t:t + 1].bitcast(u32), axis=0)).then_inc(yg_in[t], 16)

        @block.tensor
        def _(pe):
            pe.wait_ge(c_in, 16)
            pe.wait_ge(kl_in, 16)
            nc.tensor.transpose(T[0][:, 0:B], kl_rows[:, :], ident[0:B, 0:B]).then_inc(ktl_tr, 1)
            pe.wait_ge(ktl_all, 1)
            pe.wait_ge(pk_ready, 1)
            pe.wait_ge(w_in, 16)

            def group(G, u, cur, nxt, prev):
                w = 1 - u
                for s in range(GB):
                    n = 4 * G + s
                    if cur:
                        if s == 0:
                            pe.wait_ge(mb_ready, G + 1)
                            pe.wait_ge(ktl_ready, G + 1)
                        if s in (0, 2):
                            pe.wait_ge(kt_ready, 2 * G + 1 + s // 2)
                        pe.wait_ge(qb_ready, n + 1)
                        for g in range(4):
                            after(pe, exp_done, 4 * n - 3 + g)
                            nc.tensor.matmul(R[:, g, 0:SK], QB[u][:, s, 4 * g:4 * g + 4, :], KT[u][:, s, :], start=True, stop=False)
                            nc.tensor.matmul(R[:, g, 0:SK], pick_bf[:, s, :], MB[u][:, :], start=False, stop=True).then_inc(rows_done, 1)
                    if (cur if s else prev):
                        for kt, (tr, ev) in enumerate(((tr0, ev0), (tr1, ev1))):
                            after(pe, ev, n - 1)
                            if kt == 0:
                                pe.wait_ge(exp_done, 4 * n)
                            for g in range(4):
                                last = nc.tensor.transpose(T[kt][:, g * P:(g + 1) * P], PR[(s + 1) % 2][:, g, kt * P:(kt + 1) * P], ident)
                            last.then_inc(tr, 1)
                    if s == 0 and cur:
                        pe.wait_ge(v_in[1][u], 16 * (G + 2 - u))
                        for b in range(2):
                            for kt in range(2):
                                last = nc.tensor.transpose(M[:, (2 * b + kt) * P:(2 * b + kt + 1) * P], V[u][:, kt, b + 2, :], ident)
                        last.then_inc(kt_tr, 1)
                    if s == 1:
                        if cur:
                            pe.wait_ge(kt_ready, 2 * G + 2)
                        elif prev:
                            pe.wait_ge(x1_done, G - 1)
                    if s == 1 and nxt:
                        pe.wait_ge(xh_ready, G + 2)
                        nc.tensor.transpose(M[:, P:2 * P], XH[:, :], ident).then_inc(qt_tr, 1)
                    if s == 1 and prev:
                        pe.wait_ge(plc, 4 * G)
                        nc.tensor.transpose(M[0:16, 0:P], PLG[w][:, :], ident).then_inc(plt, 1)
                    if (cur if s >= 2 else prev):
                        pe.wait_ge(ev0, n - 1)
                        pe.wait_ge(ev1, n - 1)
                        if s == 2 and prev:
                            pe.wait_ge(osb_ready, G)
                        b = (s + 2) % 4
                        vv = V[u] if s >= 2 else V[w]
                        for kt in range(2):
                            for g in range(4):
                                last = nc.tensor.matmul(O[32 * g:32 * g + 32, b * P:(b + 1) * P], vv[:, kt, b, 32 * g:32 * g + 32],
                                                        PT[kt][s % 2][:, g * P:(g + 1) * P], start=(b == 0 and kt == 0), stop=False,
                                                        skip_group_check=True)
                        last.then_inc(pv_done, 1)
                    if s == 1 and prev:
                        pe.wait_ge(pl_ready, G)
                        pe.wait_ge(vlx_ready, G)
                        for b in range(GB):
                            last = nc.tensor.matmul(O[:, b * P:(b + 1) * P], VLX[:, b, :], PLS[:, :], start=False, stop=(b == GB - 1),
                                                    skip_group_check=True)
                        last.then_inc(left_done, 1)
                    if s == 2 and prev:
                        pe.wait_ge(a_ready, G)
                        if nxt:
                            pe.wait_ge(qt_ready, G + 2)
                        for b in range(GB):
                            last = nc.tensor.transpose(M[:, b * P:(b + 1) * P], A[:, 4 * b:4 * b + 4, :], ident)
                        last.then_inc(zm_done, 1)
                    if s == 3 and prev:
                        pe.wait_ge(om_ready, G)
                        for h in range(4):
                            last = nc.tensor.matmul(M[:, 0:D], OM[:, h, :], wout_sb[:, :], start=(h == 0), stop=(h == 3))
                        last.then_inc(y_done, 1)
                    if s == 3 and nxt:
                        after(pe, x1_done, G)
                        if not prev:
                            pe.wait_ge(qt_ready, G + 2)
                        pe.wait_ge(v_in[0][w], 16 * (G + 3 - w))
                        for b in range(2):
                            for kt in range(2):
                                last = nc.tensor.transpose(M[:, (2 * b + kt) * P:(2 * b + kt + 1) * P], V[w][:, kt, b, :], ident)
                        last.then_inc(kt_tr, 1)
            groups(pe, group)

            pe.wait_ge(bw_in, 80)

            def project_out(t, u):
                pe.wait_ge(xnt_ready, t + 1)
                after(pe, qkv_ready, t - 1)
                nc.tensor.matmul(R[:, u, 0:3 * D], XNT[u][:, :], wqkv_sb[:, :], start=True, stop=True).then_inc(qkv_done, 1)

            def project(t, u):
                pe.wait_ge(xn_ready, t + 1)
                after(pe, xnt_ready, t - 1)
                nc.tensor.transpose(T[u][:, 0:P], XN[u][:, :], ident).then_inc(xn_tr, 1)
                if not (isinstance(t, int) and t == 0):
                    project_out(t - 1, 1 - u)
            tiles(pe, project)
            project_out(NT - 1, 1)
            pe.wait_ge(qkv_ready, NT)

            def attend(t, u, cur=True, mid=True, last_out=True):
                v = 1 - u
                if cur:
                    pe.wait_ge(qkr_ready, 2 * (t + 1))
                if mid:
                    pe.wait_ge(ks_ready, t)
                    pe.wait_ge(qs_ready, 4 * t)
                    after(pe, om2_ready, t - 1)
                if cur:
                    nc.tensor.transpose(T[0][:, 0:P], QKR[u][:, D:2 * D], ident)
                    nc.tensor.transpose(T[1][:, 0:P], QKR[u][:, 0:D], ident).then_inc(qk_tr, 1)
                if mid:
                    for b in range(GB):
                        for g in range(4):
                            last = nc.tensor.matmul(R[32 * b:32 * b + 32, g, 0:P], KS[v][32 * g:32 * g + 32, 32 * b:32 * b + 32],
                                                    QS[v][32 * g:32 * g + 32, b, :], start=True, stop=True)
                    last.then_inc(s_done, 1)
                if last_out:
                    pe.wait_ge(om2_ready, t - 1)
                    after(pe, x2_done, t - 2)
                if mid:
                    pe.wait_ge(vs_ready, t)
                    pe.wait_ge(pm_ready, t)
                if last_out:
                    for h in range(4):
                        last = nc.tensor.matmul(M[:, 0:D], OM2[u][:, h, :], wo_sb[:, :], start=(h == 0), stop=(h == 3))
                    last.then_inc(y2_done, 1)
                if mid:
                    for b in range(GB):
                        for g in range(4):
                            last = nc.tensor.matmul(R[32 * g:32 * g + 32, b, 0:P], VS[v][32 * b:32 * b + 32, 32 * g:32 * g + 32],
                                                    PM[v][32 * b:32 * b + 32, g, :], start=True, stop=True)
                    last.then_inc(z_done, 1)
            attend(0, 0, mid=False, last_out=False)
            attend(1, 1, last_out=False)
            with pe.Fori(1, NT // 2) as i:
                attend(2 * i, 0)
                attend(2 * i + 1, 1)
            attend(NT, 0, cur=False)
            attend(NT + 1, 1, cur=False, mid=False)

            def logits(t, u):
                pe.wait_ge(xmt_ready, t + 1)
                nc.tensor.matmul(O[:, ds(E * t, E)], XNT[u][:, :], wr_sb[:, :], start=True, stop=True).then_inc(lg_done, 1)

            def route(t, u):
                pe.wait_ge(xm_ready, 2 * t + 1)
                after(pe, xmt_ready, t - 1)
                nc.tensor.transpose(T[u][:, 0:P], XN[u][:, :], ident).then_inc(xm_tr, 1)
                if not (isinstance(t, int) and t == 0):
                    logits(t - 1, 1 - u)
            tiles(pe, route)
            logits(NT - 1, 1)
            pe.wait_ge(oh_ready, 1)
            onehot = OH[:, :, :].rearrange("p t e -> p (t e)")
            nc.tensor.matmul(M[:, 0:NT * E], const("before"), onehot, start=True, stop=True)
            nc.tensor.matmul(T[0][:, 0:NT * E], const("ones"), onehot, start=True, stop=True).then_inc(cnt_done, 1)
            pe.wait_ge(wexp_in, 96)
            pe.wait_ge(te_ready, 1)

            def take(j, u):
                pe.wait_ge(xs_in[u], 8 * (j + 2 - u))
                after(pe, xst_ready, j - 1)
                nc.tensor.transpose(T[u][:, 0:P], XS[u][:, :], ident).then_inc(xs_tr, 1)

            def up(j, u):
                e = pe.value_load(te[0:1, one(j)], min_val=0, max_val=E - 1)
                pe.wait_ge(xst_ready, j + 1)
                after(pe, hb_ready, j - 1)
                nc.tensor.matmul(R[:, u, :], XST[u][:, :], W1S[:, one(e), :], start=True, stop=True).then_inc(up_done, 1)

            def down(j, u):
                e = pe.value_load(te[0:1, one(j)], min_val=0, max_val=E - 1)
                pe.wait_ge(hg_ready, j + 1)
                after(pe, ht_ready, j - 1)
                for c in range(FC):
                    last = nc.tensor.transpose(R[:, 2 + u, c * P:(c + 1) * P], HGL[u][:, c * P:(c + 1) * P], ident)
                last.then_inc(ht_tr, 1)
                pe.wait_ge(ht_ready, j + 1)
                after(pe, ys_ready, j - 1)
                for c in range(FC):
                    last = nc.tensor.matmul((O, M)[u][:, 0:D], HT[u][:, c, :], W2S[:, ds(FC * e + c, 1), :], start=(c == 0), stop=(c == FC - 1))
                last.then_inc(down_done, 1)

            def expert(j, u):
                take(j, u)
                up(j, u)
                if not (isinstance(j, int) and j == 0):
                    down(j - 1, 1 - u)
            tiles(pe, expert, ET)
            down(ET - 1, 0)


def build(nc, arrays):
    ap = {}
    for name, a in arrays.items():
        ap[name] = nc.dram_tensor(name, a.shape, mybir.dt.from_np(a.dtype), kind="ExternalInput").ap()
    out = nc.dram_tensor("out_0_dram", (B, S, D), mybir.dt.float32, kind="ExternalOutput").ap()
    xs = nc.dram_tensor("xs_scratch", (ET * P, D), mybir.dt.float32, kind="Internal").ap()
    ys = nc.dram_tensor("ys_scratch", (ET * P, D), mybir.dt.float32, kind="Internal").ap()
    perceiver_block(nc, *(ap[n] for n in arrays), out, xs, ys)


def lay_out(i):
    c = np.ascontiguousarray
    a = {k: np.asarray(v) for k, v in i.items()}
    return {
        "x_dram": c(a["x"]), "ctx_dram": c(a["ctx_1024"]), "mask_dram": c(a["mask_Bx1xSxS2_ik1"]),
        "w_out_t_dram": c(a["L0_xattn_w_out"].T), "b_out_dram": c(a["L0_xattn_b_out"]),
        "wqkv_t_dram": c(np.concatenate([a["L0_attn_Wq"].T, a["L0_attn_Wk"].T, a["L0_attn_Wv"].T], axis=1)),
        "bqkv_dram": c(np.concatenate([a["L0_attn_bq"], a["L0_attn_bk"], a["L0_attn_bv"]])),
        "wo_t_dram": c(a["L0_attn_Wo"].T), "norm_w_dram": c(a["L0_attn_norm_w"]),
        "wr_dram": c(a["L0_ffn_Wr"]), "w1_dram": c(a["L0_ffn_W1"]), "b1_dram": c(a["L0_ffn_b1"]),
        "w2_dram": c(a["L0_ffn_W2"]), "b2_dram": c(a["L0_ffn_b2"]), "const_dram": const_table(),
    }


def kernel(**inputs):
    import concourse.bacc as bacc
    from concourse.bass_utils import run_bass_kernel_spmd

    nc = bacc.Bacc("TRN2", target_bir_lowering=False, num_devices=1)
    arrays = lay_out(inputs)
    build(nc, arrays)
    r = run_bass_kernel_spmd(nc, [arrays], core_ids=[0])
    return r.results[0]["out_0_dram"]
```
